# Optimizing a Trainium2 kernel written in Bass

```python
import numpy as np
import jax
import jax.numpy as jnp

def _softmax(x, axis=-1):
    return jax.nn.softmax(x, axis=axis)

def _gelu(x):
    return jax.nn.gelu(x, approximate=True)

def _silu(x):
    return jax.nn.silu(x)

def _sigmoid(x):
    return jax.nn.sigmoid(x)

def _layernorm(x, axis=-1, eps=1e-05):
    m = jnp.mean(x, axis=axis, keepdims=True)
    v = jnp.var(x, axis=axis, keepdims=True)
    return (x - m) / jnp.sqrt(v + eps)

def _scatter_add(tgt, idx, src, axis=0):
    return tgt.at[idx].add(src)

def _segment_sum(src, seg, n):
    return jax.ops.segment_sum(src, seg, n)
kernel_name = 'mk_rec_standalone_d1_rec_r8_e4d2de'

def setup_inputs(seed: int=0):
    np.random.seed(seed)
    _w = jnp.asarray

    def _rec_inputs():
        import jax
        import jax.numpy as jnp
        _rk = jax.random.key(seed)
        r_x = -0.000292821 + 1.00034 * jax.random.normal(jax.random.fold_in(_rk, 1), (2048, 1024), jnp.float32)
        return r_x
    r_x = _rec_inputs()

    def _L0_rec_setup():
        import jax, jax.numpy as jnp
        import numpy as np
        B, D, H, E, T, HT = (512, 1024, 1024, 8, 4, 512)
        key = jax.random.key(seed)
        ks = jax.random.split(key, 5)
        s = lambda fan_in: 1.0 / np.sqrt(fan_in)
        x = jax.random.normal(ks[0], (B, D), dtype=jnp.float32)
        We = jax.random.uniform(ks[1], (E, H, D), dtype=jnp.float32, minval=-s(D), maxval=s(D))
        Wg = jax.random.uniform(ks[2], (T, E, D), dtype=jnp.float32, minval=-s(D), maxval=s(D))
        Wt1 = jax.random.uniform(ks[3], (T, HT, H), dtype=jnp.float32, minval=-s(H), maxval=s(H))
        Wt2 = jax.random.uniform(ks[4], (T, HT), dtype=jnp.float32, minval=-s(HT), maxval=s(HT))
        return {'x': x, 'We': We, 'Wg': Wg, 'Wt1': Wt1, 'Wt2': Wt2}
    _L0_rec_all = _L0_rec_setup()
    _L0_rec_in = {k: v for k, v in _L0_rec_all.items() if k in ('We', 'Wg', 'Wt1', 'Wt2')}
    del _L0_rec_all
    return {'r_x': r_x, 'L0_rec_We': _L0_rec_in['We'], 'L0_rec_Wg': _L0_rec_in['Wg'], 'L0_rec_Wt1': _L0_rec_in['Wt1'], 'L0_rec_Wt2': _L0_rec_in['Wt2']}

def reference(r_x, L0_rec_We, L0_rec_Wg, L0_rec_Wt1, L0_rec_Wt2):
    import jax
    import jax.numpy as jnp

    def _L0_rec_ref(x, We, Wg, Wt1, Wt2):
        import jax, jax.numpy as jnp
        import numpy as np
        B, D, H, E, T, HT = (512, 1024, 1024, 8, 4, 512)
        expert_out = jax.nn.relu(jnp.einsum('bd,ehd->bhe', x, We))
        gate = jax.nn.softmax(jnp.einsum('bd,ted->bet', x, Wg), axis=1)
        gated = jnp.einsum('bhe,bet->bht', expert_out, gate)
        h1 = jax.nn.relu(jnp.einsum('bht,tkh->bkt', gated, Wt1))
        out = jnp.einsum('bkt,tk->bt', h1, Wt2)
        return out
    y = _L0_rec_ref(r_x, L0_rec_We, L0_rec_Wg, L0_rec_Wt1, L0_rec_Wt2)
    return y

_drawn_inputs = setup_inputs


def setup_inputs(seed=0):
    import zlib

    import numpy as np

    out = dict(_drawn_inputs(seed))
    spreads = {}
    factors = {}
    for name, (base, spread) in spreads.items():
        noise = np.random.default_rng([zlib.crc32(name.encode()), seed]).standard_normal(out[name].shape)
        drawn = base * np.exp(spread * noise) if base else spread * noise
        out[name] = jnp.asarray(drawn.astype(out[name].dtype))
    for name, factor in factors.items():
        out[name] = (out[name] * factor).astype(out[name].dtype)
    return out
```

```python
from contextlib import ExitStack

import concourse.bass as bass
from concourse import mybir

F32 = mybir.dt.float32
F32R = mybir.dt.float32r
ALU = mybir.AluOpType
ACT = mybir.ActivationFunctionType
AX_X = mybir.AxisListType.X

P = 128
N = 512
PIECES = 4


def mmoe_kernel(nc, x, we, wg, wt1, wt2, out):
    CHUNKS, _, KT, ROWS = x.shape
    HALVES = 2
    EXPERTS = we.shape[0] // HALVES
    TASKS = wt1.shape[0]
    TILES = ROWS // P
    EXPERT_STEPS = EXPERTS * HALVES
    STEPS = EXPERT_STEPS + TASKS
    UNITS = STEPS * TILES
    TURNS = TASKS * TILES
    GATES = TASKS * EXPERTS
    KP = KT // PIECES
    KH = KT // 2

    we_rows = we.rearrange("s p k n -> (s p) (k n)")
    wt1_rows = wt1.rearrange("s p k n -> (s p) (k n)")
    x_rows = x.rearrange("c p k n -> (c p) (k n)")

    with ExitStack() as ctx:
        def sb(name, shape, dt=F32):
            return ctx.enter_context(nc.sbuf_tensor(name, shape, dt))

        def sem(name):
            return ctx.enter_context(nc.semaphore(name))

        raw = [sb(f"raw{h}", [P, KH, N]) for h in range(2)]
        x_high = sb("x_high", [P, KT, ROWS], F32R)
        x_low = sb("x_low", [P, KT, ROWS], F32R)
        slab_high = [sb(f"slab_high{b}", [P, KT, N], F32R) for b in range(2)]
        slab_low = [sb(f"slab_low{b}", [P, KT, N], F32R) for b in range(2)]
        gated = sb("gated", [P, TILES, TASKS, HALVES * N])
        x0_raw = gated[:, 0, :, :].rearrange("p t (a n) -> p (t a) n", n=ROWS)
        gt_high = [sb(f"gt_high{b}", [P, KT, P], F32R) for b in range(2)]
        gt_low = [sb(f"gt_low{b}", [P, KT, P], F32R) for b in range(2)]
        wg_raw = sb("wg_raw", [P, KT, GATES])
        wg_split = sb("wg_split", [P, KT, P], F32R)
        wt2_all = sb("wt2_all", [P, TASKS, N])
        ident = sb("ident", [P, P])
        fold = sb("fold", [2 * GATES, GATES])
        top = sb("top", [P, TURNS])
        shifted = sb("shifted", [P, TURNS, EXPERTS])
        expd = sb("expd", [P, TURNS, EXPERTS])
        total = sb("total", [P, TURNS])
        inv = sb("inv", [P, TURNS])
        gate = sb("gate", [P, TURNS, EXPERTS])
        result = sb("result", [P, TURNS])
        results = sb("results", [P, CHUNKS * TURNS])

        z = [ctx.enter_context(nc.psum_tensor(f"z{i}", [P, N], F32)) for i in range(TILES)]
        turn = [ctx.enter_context(nc.psum_tensor(f"turn{b}", [P, KT, P], F32)) for b in range(2)]
        parts_ps = turn[0][:, 0:ROWS // P, :].rearrange("p a b -> p (a b)")
        logits_ps = turn[1][:, 0, :].rearrange("p (g e) -> p g e", e=EXPERTS)
        parts = gated[0:2 * GATES, TILES - 1, 0, 0:ROWS].rearrange("g (i r) -> g i r", r=P)

        raw_in = [sem(f"raw_in{h}") for h in range(2)]
        x0_in = [sem(f"x0_in{q}") for q in range(PIECES)]
        wg_in = sem("wg_in")
        wt2_in = sem("wt2_in")
        ident_zero = sem("ident_zero")
        ident_made = sem("ident_made")
        wg_zero = sem("wg_zero")
        wg_high_made = sem("wg_high_made")
        wg_low_made = sem("wg_low_made")
        fold_made = sem("fold_made")
        high_made = sem("high_made")
        low_made = sem("low_made")
        x_high_made = sem("x_high_made")
        x_low_made = sem("x_low_made")
        chunk_begun = sem("chunk_begun")
        parts_done = sem("parts_done")
        parts_copied = sem("parts_copied")
        logits_done = sem("logits_done")
        shifted_made = sem("shifted_made")
        expd_made = sem("expd_made")
        chain = sem("chain")
        unit_done = sem("unit_done")
        relu_made = sem("relu_made")
        unit_read = sem("unit_read")
        turned = sem("turned")
        gt_high_made = sem("gt_high_made")
        gt_low_made = sem("gt_low_made")
        gathered = sem("gathered")
        stored = sem("stored")

        block = ctx.enter_context(nc.Block())

        @block.sync
        def _(sp):
            def load_half(src, row, h):
                return sp.dma_start(raw[h][:, :, :].rearrange("p k n -> p (k n)"),
                                    src[bass.ds(row, P), h * KH * N:(h + 1) * KH * N]).then_inc(raw_in[h], 16)

            def load(src, row, slabs_before):
                for h in range(2):
                    sp.wait_ge(low_made, (slabs_before - 1) * PIECES + 2 * (h + 1))
                    load_half(src, row, h)

            def slabs(c):
                with sp.Fori(1, EXPERT_STEPS) as j:
                    load(we_rows, j * P, c * STEPS + j)
                with sp.Fori(0, TASKS) as t:
                    load(wt1_rows, t * P, c * STEPS + EXPERT_STEPS + t)

            x0_flat = x0_raw.rearrange("p k n -> p (k n)")

            def load_x0(q):
                piece = slice(q * KP * ROWS, (q + 1) * KP * ROWS)
                sp.dma_start(x0_flat[:, piece], x_rows[0:P, piece]).then_inc(x0_in[q], 16)

            load_x0(0)
            load_half(we_rows, 0, 0)
            sp.dma_start(wg_raw[:, :, :], wg).then_inc(wg_in, 16)
            for q in range(1, PIECES):
                load_x0(q)
            load_half(we_rows, 0, 1)
            sp.dma_start(wt2_all[:, :, :], wt2.partition_broadcast(P)).then_inc(wt2_in, 16)
            with sp.Fori(0, CHUNKS - 1) as c:
                slabs(c)
                load(x_rows, (c + 1) * P, (c + 1) * STEPS)
                for h in range(2):
                    sp.wait_ge(x_low_made, (c + 1) * PIECES + 2 * (h + 1))
                    load_half(we_rows, 0, h)
            slabs(CHUNKS - 1)
            sp.wait_ge(gathered, CHUNKS)
            sp.dma_start(out, results[:, :]).then_inc(stored, 16)
            sp.wait_ge(stored, 16)

        def low_of(eng, low, high, value, q):
            return eng.tensor_tensor(low[:, q * KP:(q + 1) * KP, :], value,
                                     high[:, q * KP:(q + 1) * KP, :].bitcast(F32), ALU.subtract)

        def raw_piece(q):
            at = q * KP % KH
            return raw[q * KP // KH][:, at:at + KP, :]

        @block.gpsimd
        def _(pool):
            nc.gpsimd.memset(wg_split[:, :, 2 * GATES:].bitcast(F32), 0.0).then_inc(wg_zero, 1)
            nc.gpsimd.memset(ident[:, :], 0.0).then_inc(ident_zero, 1)
            pool.wait_ge(ident_zero, 1)
            nc.gpsimd.affine_select(out=ident[:, :], in_=ident[:, :], compare_op=ALU.not_equal, fill=1.0,
                                    base=0, pattern=[[-1, P]], channel_multiplier=1).then_inc(ident_made, 1)

            def slab_lows(s, b):
                for q in range(PIECES):
                    pool.wait_ge(high_made, s * PIECES + q + 1)
                    low_of(nc.gpsimd, slab_low[b], slab_high[b], raw_piece(q), q).then_inc(low_made, 1)

            def chunk_lows(c):
                with pool.Fori(0, STEPS // 2) as i:
                    for b in range(2):
                        slab_lows(c * STEPS + i * 2 + b, b)

            with pool.Fori(0, CHUNKS - 1) as c:
                chunk_lows(c)
                for q in range(PIECES):
                    pool.wait_ge(x_high_made, (c + 1) * PIECES + q + 1)
                    low_of(nc.gpsimd, x_low, x_high, raw_piece(q), q).then_inc(x_low_made, 1)
            chunk_lows(CHUNKS - 1)

        @block.scalar
        def _(act):
            def high_of(high, value, q):
                return nc.scalar.activation(high[:, q * KP:(q + 1) * KP, :], value, ACT.Copy)

            def half_loaded(h, n):
                act.wait_ge(raw_in[h], n * 16)

            def slab_highs(c, j, b, halves=(0, 1)):
                for h in halves:
                    half_loaded(h, c * (STEPS + 1) + j + 1)
                    for q in range(h * 2, h * 2 + 2):
                        high_of(slab_high[b], raw_piece(q), q).then_inc(high_made, 1)

            def next_x_highs(c, h):
                half_loaded(h, (c + 1) * (STEPS + 1))
                for q in range(h * 2, h * 2 + 2):
                    high_of(x_high, raw_piece(q), q).then_inc(x_high_made, 1)

            def relu(c, j, i):
                act.wait_ge(unit_done, c * UNITS + j * TILES + i + 1)
                nc.scalar.activation(z[i][:, :], z[i][:, :], ACT.Relu).then_inc(relu_made, 1)

            def round_turned(c, t, i):
                act.wait_ge(unit_done, c * UNITS + (EXPERT_STEPS + t) * TILES + i - 1)
                act.wait_ge(turned, c * TURNS + t * TILES + i + 1)
                nc.scalar.activation(gt_high[i % 2][:, :, :], turn[i % 2][:, :, :],
                                     ACT.Copy).then_inc(gt_high_made, 1)

            def experts(c):
                act.wait_ge(chunk_begun, c + 1)
                slab_highs(c, 1, 1)
                act.wait_ge(shifted_made, c + 1)
                nc.scalar.activation(expd[:, :, :], shifted[:, :, :], ACT.Exp).then_inc(expd_made, 1)
                for i in range(TILES):
                    relu(c, 0, i)
                with act.Fori(0, EXPERTS - 1) as e:
                    for half in range(HALVES):
                        j = e * HALVES + half + 1
                        act.wait_ge(unit_done, c * UNITS + j * TILES)
                        slab_highs(c, j + 1, half)
                        for i in range(TILES):
                            relu(c, j, i)
                j = EXPERT_STEPS - 1
                act.wait_ge(unit_done, c * UNITS + j * TILES)
                slab_highs(c, j + 1, 0)
                for i in range(TILES):
                    if i == TILES - 1:
                        round_turned(c, 0, 0)
                    relu(c, j, i)

            def towers(c, last):
                for t in range(TASKS):
                    j = EXPERT_STEPS + t
                    if t < TASKS - 1:
                        act.wait_ge(unit_done, c * UNITS + j * TILES)
                        slab_highs(c, j + 1, (j + 1) % 2)
                    for i in range(TILES):
                        if (t, i) < (TASKS - 1, TILES - 1):
                            round_turned(c, t + (i + 1) // TILES, (i + 1) % TILES)
                        if not last and t == TASKS - 2 and i >= TILES - 2:
                            next_x_highs(c, i - (TILES - 2))
                        if not last and t == TASKS - 1 and i < 2:
                            slab_highs(c + 1, 0, 0, halves=(i,))

            def x0_highs(q):
                act.wait_ge(x0_in[q], 16)
                high_of(x_high, x0_raw[:, q * KP:(q + 1) * KP, :], q).then_inc(x_high_made, 1)

            x0_highs(0)
            slab_highs(0, 0, 0, halves=(0,))
            act.wait_ge(wg_in, 16)
            nc.scalar.activation(wg_split[:, :, 0:GATES], wg_raw[:, :, :], ACT.Copy).then_inc(wg_high_made, 1)
            for q in range(1, PIECES):
                x0_highs(q)
            slab_highs(0, 0, 0, halves=(1,))
            with act.Fori(0, CHUNKS - 1) as c:
                experts(c)
                towers(c, last=False)
            experts(CHUNKS - 1)
            towers(CHUNKS - 1, last=True)

        @block.tensor
        def _(pe):
            def product(i, k, left_high, left_low, b):
                right_high, right_low = slab_high[b][:, k, :], slab_low[b][:, k, :]
                first = nc.tensor.matmul(z[i][:, :], left_high, right_high, start=(k == 0), stop=False)
                nc.tensor.matmul(z[i][:, :], left_high, right_low, start=False, stop=False)
                last = nc.tensor.matmul(z[i][:, :], left_low, right_high, start=False, stop=(k == KT - 1))
                return first, last

            def expert_product(i, k, b):
                rows = slice(i * P, (i + 1) * P)
                return product(i, k, x_high[:, k, rows], x_low[:, k, rows], b)

            def expert_unit(i, b):
                for k in range(KT):
                    _, last = expert_product(i, k, b)
                last.then_inc(unit_done, 1)

            def tower_unit(i, b):
                for k in range(KT):
                    _, last = product(i, k, gt_high[i % 2][:, k, :], gt_low[i % 2][:, k, :], b)
                last.then_inc(unit_done, 1)

            def slab_split(c, j, q=PIECES - 1):
                pe.wait_ge(low_made, (c * STEPS + j) * PIECES + q + 1)

            def x_split(c, q):
                pe.wait_ge(x_low_made, c * PIECES + q + 1)

            def bank_free(c, j, i):
                pe.wait_ge(unit_read, c * UNITS + j * TILES + i + 1)

            def gate_parts(c):
                x_split(c, PIECES - 1)
                for k in range(KT):
                    nc.tensor.matmul(parts_ps, wg_split[:, k, :], x_high[:, k, :], start=(k == 0), stop=False)
                    last = nc.tensor.matmul(parts_ps, wg_split[:, k, :], x_low[:, k, :],
                                            start=False, stop=(k == KT - 1))
                last.then_inc(parts_done, 1)

            def gate_logits(c):
                pe.wait_ge(parts_copied, c + 1)
                for i in range(TILES):
                    last = nc.tensor.matmul(turn[1][:, 0, i * GATES:(i + 1) * GATES], parts[:, i, :], fold[:, :],
                                            start=True, stop=True)
                last.then_inc(logits_done, 1)

            def first_step(c):
                for q in range(PIECES):
                    x_split(c, q)
                    slab_split(c, 0, q)
                    for i in range(TILES):
                        if q == 0:
                            bank_free(c, 0, i)
                        for k in range(q * KP, (q + 1) * KP):
                            first, last = expert_product(i, k, 0)
                            if (i, k) == (0, 0):
                                first.then_inc(chunk_begun, 1)
                        if q == PIECES - 1:
                            last.then_inc(unit_done, 1)
                    if q == 0:
                        gate_parts(c)
                    if q == 1:
                        gate_logits(c)

            def transposes(c, t, i):
                if t == 0:
                    pe.wait_ge(unit_read, c * UNITS + EXPERT_STEPS * TILES + i + 1)
                if (t, i) > (0, 1):
                    pe.wait_ge(gt_low_made, c * TURNS + t * TILES + i - 1)
                for k in range(KT):
                    last = nc.tensor.transpose(turn[i % 2][:, k, :], gated[:, i, t, k * P:(k + 1) * P],
                                               ident[:, :])
                last.then_inc(turned, 1)

            pe.wait_ge(ident_made, 1)
            pe.wait_ge(wg_zero, 1)
            pe.wait_ge(wg_low_made, 1)
            pe.wait_ge(fold_made, 1)
            with pe.Fori(0, CHUNKS) as c:
                first_step(c)
                with pe.Fori(0, EXPERTS - 1) as e:
                    for half in range(HALVES):
                        j = e * HALVES + half + 1
                        slab_split(c, j)
                        for i in range(TILES):
                            bank_free(c, j, i)
                            expert_unit(i, (half + 1) % 2)
                j = EXPERT_STEPS - 1
                slab_split(c, j)
                for i in range(TILES):
                    if i == TILES - 1:
                        transposes(c, 0, 0)
                    bank_free(c, j, i)
                    expert_unit(i, j % 2)
                for t in range(TASKS):
                    slab_split(c, EXPERT_STEPS + t)
                    for i in range(TILES):
                        if (t, i) < (TASKS - 1, TILES - 1):
                            transposes(c, t + (i + 1) // TILES, (i + 1) % TILES)
                        pe.wait_ge(gt_low_made, c * TURNS + t * TILES + i + 1)
                        bank_free(c, EXPERT_STEPS + t, i)
                        tower_unit(i, t % 2)

        @block.vector
        def _(dve):
            LINKS = 4

            def wide(v):
                return v[:, :].rearrange("p (g o) -> p g o", o=1).to_broadcast([P, TURNS, EXPERTS])

            def softmax(c):
                dve.wait_ge(parts_done, c + 1)
                nc.vector.tensor_copy(parts, parts_ps[0:2 * GATES, :].rearrange("g (i r) -> g i r", r=P)
                                      ).then_inc(parts_copied, 1)
                dve.wait_ge(logits_done, c + 1)
                nc.vector.tensor_reduce(top[:, :], logits_ps, AX_X, ALU.max).then_inc(chain, 1)
                dve.wait_ge(chain, c * LINKS + 1)
                nc.vector.tensor_tensor(shifted[:, :, :], logits_ps, wide(top),
                                        ALU.subtract).then_inc(shifted_made, 1)
                dve.wait_ge(expd_made, c + 1)
                nc.vector.tensor_reduce(total[:, :], expd[:, :, :], AX_X, ALU.add).then_inc(chain, 1)
                dve.wait_ge(chain, c * LINKS + 2)
                nc.vector.reciprocal(inv[:, :], total[:, :]).then_inc(chain, 1)
                dve.wait_ge(chain, c * LINKS + 3)
                nc.vector.tensor_tensor(gate[:, :, :], expd[:, :, :], wide(inv), ALU.mult).then_inc(chain, 1)
                dve.wait_ge(chain, c * LINKS + 4)

            def add_expert(c, j, e, half, i, first=False):
                dve.wait_ge(relu_made, c * EXPERT_STEPS * TILES + j * TILES + i + 1)
                if not first:
                    dve.wait_ge(unit_read, c * UNITS + (j - HALVES + 1) * TILES + i + 1)
                for t in range(TASKS):
                    acc = gated[:, i, t, half * N:(half + 1) * N]
                    g = gate[:, i * TASKS + t, bass.ds(e, 1)]
                    if first:
                        last = nc.vector.tensor_scalar(acc, z[i][:, :], g, None, ALU.mult)
                    else:
                        last = nc.vector.scalar_tensor_tensor(out=acc, in0=z[i][:, :], scalar=g, in1=acc,
                                                              op0=ALU.mult, op1=ALU.add)
                last.then_inc(unit_read, 1)

            def low_turned(c, t, i):
                dve.wait_ge(gt_high_made, c * TURNS + t * TILES + i + 1)
                nc.vector.tensor_tensor(gt_low[i % 2][:, :, :], turn[i % 2][:, :, :],
                                        gt_high[i % 2][:, :, :].bitcast(F32), ALU.subtract).then_inc(gt_low_made, 1)

            def head(c, t, i):
                dve.wait_ge(unit_done, c * UNITS + (EXPERT_STEPS + t) * TILES + i + 1)
                nc.vector.scalar_tensor_tensor(out=z[i][:, :], in0=z[i][:, :], scalar=0.0, in1=wt2_all[:, t, :],
                                               op0=ALU.max, op1=ALU.mult,
                                               accum_out=result[:, i * TASKS + t:i * TASKS + t + 1]
                                               ).then_inc(unit_read, 1)

            nc.vector.memset(results[:, :], 0.0).then_inc(unit_read, TILES)
            dve.wait_ge(ident_made, 1)
            nc.vector.tensor_tensor(fold[:, :], ident[0:2 * GATES, 0:GATES], ident[0:2 * GATES, GATES:2 * GATES],
                                    ALU.add).then_inc(fold_made, 1)

            def x0_low(q):
                dve.wait_ge(x_high_made, q + 1)
                low_of(nc.vector, x_low, x_high, x0_raw[:, q * KP:(q + 1) * KP, :], q).then_inc(x_low_made, 1)

            x0_low(0)
            dve.wait_ge(wg_high_made, 1)
            nc.vector.tensor_tensor(wg_split[:, :, GATES:2 * GATES], wg_raw[:, :, :],
                                    wg_split[:, :, 0:GATES].bitcast(F32), ALU.subtract).then_inc(wg_low_made, 1)
            for q in range(1, PIECES):
                x0_low(q)
            dve.wait_ge(wt2_in, 16)
            with dve.Fori(0, CHUNKS) as c:
                softmax(c)
                for half in range(HALVES):
                    for i in range(TILES):
                        add_expert(c, half, 0, half, i, first=True)
                with dve.Fori(1, EXPERTS - 1) as e:
                    for half in range(HALVES):
                        for i in range(TILES):
                            add_expert(c, e * HALVES + half, e, half, i)
                for half in range(HALVES):
                    for i in range(TILES):
                        if half == HALVES - 1 and i == TILES - 1:
                            low_turned(c, 0, 0)
                        add_expert(c, EXPERT_STEPS - HALVES + half, EXPERTS - 1, half, i)
                for t in range(TASKS):
                    for i in range(TILES):
                        if (t, i) < (TASKS - 1, TILES - 1):
                            low_turned(c, t + (i + 1) // TILES, (i + 1) % TILES)
                        head(c, t, i)
                dve.wait_ge(unit_read, (c + 1) * UNITS + TILES)
                nc.vector.tensor_copy(results[:, bass.ds(c * TURNS, TURNS)], result[:, :]).then_inc(gathered, 1)


def kernel(r_x, L0_rec_We, L0_rec_Wg, L0_rec_Wt1, L0_rec_Wt2):
    import numpy as np
    import concourse.bacc as bacc
    from concourse.bass_utils import run_bass_kernel_spmd

    rows, width = np.shape(r_x)
    experts, hidden, _ = np.shape(L0_rec_We)
    tasks, tower, _ = np.shape(L0_rec_Wt1)
    kt, ht, chunks, halves = width // 128, hidden // 128, rows // 512, hidden // 512

    arrays = {
        "x": np.asarray(r_x).reshape(chunks, 512, kt, 128).transpose(0, 3, 2, 1),
        "we": np.asarray(L0_rec_We).reshape(experts * halves, 512, kt, 128).transpose(0, 3, 2, 1),
        "wg": np.asarray(L0_rec_Wg).reshape(tasks * experts, kt, 128).transpose(2, 1, 0),
        "wt1": np.asarray(L0_rec_Wt1).reshape(tasks, tower, ht, 128).transpose(0, 3, 2, 1),
        "wt2": np.asarray(L0_rec_Wt2),
    }
    arrays = {n: np.ascontiguousarray(a) for n, a in arrays.items()}
    nc = bacc.Bacc("TRN2", target_bir_lowering=False, num_devices=1)
    args = [nc.dram_tensor(n, a.shape, mybir.dt.from_np(a.dtype), kind="ExternalInput").ap()
            for n, a in arrays.items()]
    out = nc.dram_tensor("out", (128, rows // 128 * tasks), F32, kind="ExternalOutput").ap()
    by_name = dict(zip(arrays, args))
    mmoe_kernel(nc, by_name["x"], by_name["we"], by_name["wg"], by_name["wt1"], by_name["wt2"], out)
    got = run_bass_kernel_spmd(nc, [arrays], core_ids=[0]).results[0]["out"]
    return got.reshape(128, rows // 128, tasks).transpose(1, 0, 2).reshape(rows, tasks)
```

```python
from contextlib import ExitStack

import concourse.bass as bass
from concourse import mybir

F32 = mybir.dt.float32
F32R = mybir.dt.float32r
ALU = mybir.AluOpType
ACT = mybir.ActivationFunctionType
AX_X = mybir.AxisListType.X

P = 128
N = 512
B = 32
PIECES = 4


def mmoe_kernel(nc, x, we, wg, wt1, wt2, out):
    CHUNKS, _, KT, ROWS = x.shape
    HALVES = 2
    EXPERTS = we.shape[0] // HALVES
    TASKS = wt1.shape[0]
    TILES = ROWS // P
    EXPERT_STEPS = EXPERTS * HALVES
    STEPS = EXPERT_STEPS + TASKS
    UNITS = STEPS * TILES
    TURNS = TASKS * TILES
    GATES = TASKS * EXPERTS
    RING = 4
    KP = KT // PIECES
    KH = KT // 2

    we_rows = we.rearrange("s p k n -> (s p) (k n)")
    wt1_rows = wt1.rearrange("s p k n -> (s p) (k n)")
    x_rows = x.rearrange("c p k n -> (c p) (k n)")

    with ExitStack() as ctx:
        def sb(name, shape, dt=F32):
            return ctx.enter_context(nc.sbuf_tensor(name, shape, dt))

        def sem(name):
            return ctx.enter_context(nc.semaphore(name))

        raw = [sb(f"raw{h}", [P, KH, N]) for h in range(2)]
        x_high = sb("x_high", [P, KT, ROWS], F32R)
        x_low = sb("x_low", [P, KT, ROWS], F32R)
        slab_high = [sb(f"slab_high{b}", [P, KT, N], F32R) for b in range(2)]
        slab_low = [sb(f"slab_low{b}", [P, KT, N], F32R) for b in range(2)]
        gated = sb("gated", [P, TILES, TASKS, HALVES * N])
        x0_raw = gated[:, 0, :, :].rearrange("p t (a n) -> p (t a) n", n=ROWS)
        gt_raw = [sb(f"gt_raw{b}", [P, P // B, KT, B]) for b in range(RING)]
        gt_high = [sb(f"gt_high{b}", [P, KT, P], F32R) for b in range(2)]
        gt_low = [sb(f"gt_low{b}", [P, KT, P], F32R) for b in range(2)]
        wg_raw = gated[:, 1, 0, 0:KT * GATES].rearrange("p (k g) -> p k g", g=GATES)
        wg_split = sb("wg_split", [P, KT, P], F32R)
        wt2_all = sb("wt2_all", [P, TASKS, N])
        ident = sb("ident", [2 * GATES, 2 * GATES])
        fold = sb("fold", [2 * GATES, GATES])
        top = sb("top", [P, TURNS])
        shifted = sb("shifted", [P, TURNS, EXPERTS])
        expd = sb("expd", [P, TURNS, EXPERTS])
        total = sb("total", [P, TURNS])
        inv = sb("inv", [P, TURNS])
        gate = sb("gate", [P, TURNS, EXPERTS])
        result = sb("result", [P, TURNS])
        results = sb("results", [P, CHUNKS * TURNS])

        blocks = nc.dram_tensor("blocks", (TURNS, P, HALVES * N), F32).ap()

        z = [ctx.enter_context(nc.psum_tensor(f"z{i}", [P, N], F32)) for i in range(TILES)]
        parts_ps = ctx.enter_context(nc.psum_tensor("parts_ps", [P, ROWS], F32))
        logits_ps = ctx.enter_context(nc.psum_tensor("logits_ps", [P, TURNS, EXPERTS], F32))
        parts = gated[0:2 * GATES, TILES - 1, 0, 0:ROWS].rearrange("g (i r) -> g i r", r=P)

        raw_in = [sem(f"raw_in{h}") for h in range(2)]
        x0_in = [sem(f"x0_in{q}") for q in range(PIECES)]
        slab0_in = sem("slab0_in")
        wg_in = sem("wg_in")
        wt2_in = sem("wt2_in")
        ident_zero = sem("ident_zero")
        ident_made = sem("ident_made")
        wg_zero = sem("wg_zero")
        wg_high_made = sem("wg_high_made")
        wg_low_made = sem("wg_low_made")
        fold_made = sem("fold_made")
        high_made = sem("high_made")
        low_made = sem("low_made")
        x_high_made = sem("x_high_made")
        x_low_made = sem("x_low_made")
        chunk_begun = sem("chunk_begun")
        parts_done = sem("parts_done")
        parts_copied = sem("parts_copied")
        logits_done = sem("logits_done")
        shifted_made = sem("shifted_made")
        expd_made = sem("expd_made")
        chain = sem("chain")
        unit_done = sem("unit_done")
        relu_made = sem("relu_made")
        unit_read = sem("unit_read")
        turned = sem("turned")
        blocks_out = [sem(f"blocks_out{b}") for b in range(RING)]
        blocks_in = [sem(f"blocks_in{b}") for b in range(RING)]
        gt_high_made = sem("gt_high_made")
        gt_low_made = sem("gt_low_made")
        gathered = sem("gathered")
        stored = sem("stored")

        block = ctx.enter_context(nc.Block())

        X_HIGHS = (2 * TILES + 2, 2 * TILES + 3)
        FIRST_SLAB_LOADS = (3 * TILES, 3 * TILES + 1)
        FIRST_SLAB_HIGHS = (3 * TILES + 1, 3 * TILES + 2)

        @block.sync
        def _(sp):
            def load_half(src, row, h):
                return sp.dma_start(raw[h][:, :, :].rearrange("p k n -> p (k n)"),
                                    src[bass.ds(row, P), h * KH * N:(h + 1) * KH * N]).then_inc(raw_in[h], 16)

            def load(src, row, slabs_before):
                for h in range(2):
                    sp.wait_ge(low_made, (slabs_before - 1) * PIECES + 2 * (h + 1))
                    load_half(src, row, h)

            def blocks_to_dram(c, u):
                sp.wait_ge(turned, c * TURNS + u + 1)
                sp.dma_start(blocks[u], gated[:, u % TILES, u // TILES, :]).then_inc(blocks_out[u % RING], 16)

            def blocks_to_partitions(c, u):
                sp.wait_ge(blocks_out[u % RING], (c * (TURNS // RING) + u // RING + 1) * 16)
                if u >= RING:
                    sp.wait_ge(gt_low_made, c * TURNS + u - RING + 1)
                for r in range(P // B):
                    sp.dma_start(gt_raw[u % RING][r * B:(r + 1) * B, :, :, :].rearrange("h q k i -> h q (k i)"),
                                 blocks[u].rearrange("(q h) (r c) -> r h q c", h=B, r=P // B)[r]
                                 ).then_inc(blocks_in[u % RING], 16)

            def chunk(c, last):
                with sp.Fori(1, EXPERT_STEPS) as j:
                    load(we_rows, j * P, c * STEPS + j)
                load(wt1_rows, 0, c * STEPS + EXPERT_STEPS)
                for v in range(1 - TILES, TURNS):
                    if 0 <= v + 2 < TILES:
                        blocks_to_partitions(c, v + 2)
                    if 1 <= v < TURNS - 3:
                        blocks_to_partitions(c, v + 3)
                    if v + 3 < TILES:
                        blocks_to_dram(c, v + 3)
                    if v == 0:
                        blocks_to_dram(c, TILES)
                    if 0 <= v < TURNS - 5:
                        blocks_to_dram(c, v + 5)
                    t, h = (v + TILES - 1) // TILES, (v + TILES - 1) % TILES
                    if h < 2:
                        if t + 1 < TASKS:
                            sp.wait_ge(low_made, (c * STEPS + EXPERT_STEPS + t) * PIECES + 2 * (h + 1))
                            load_half(wt1_rows, (t + 1) * P, h)
                        elif t + 1 == TASKS and not last:
                            sp.wait_ge(low_made, (c * STEPS + EXPERT_STEPS + t) * PIECES + 2 * (h + 1))
                            load_half(x_rows, (c + 1) * P, h)
                    if not last and v in FIRST_SLAB_LOADS:
                        h = FIRST_SLAB_LOADS.index(v)
                        sp.wait_ge(x_low_made, (c + 1) * PIECES + 2 * (h + 1))
                        load_half(we_rows, 0, h)

            x0_flat = x0_raw.rearrange("p k n -> p (k n)")

            def load_x0(q):
                piece = slice(q * KP * ROWS, (q + 1) * KP * ROWS)
                sp.dma_start(x0_flat[:, piece], x_rows[0:P, piece]).then_inc(x0_in[q], 16)

            load_x0(0)
            for q in range(2):
                piece = slice(q * KP * N, (q + 1) * KP * N)
                sp.dma_start(raw[0][:, :, :].rearrange("p k n -> p (k n)")[:, piece],
                             we_rows[0:P, piece]).then_inc([slab0_in, raw_in[0]][q], 16)
            sp.dma_start(wg_raw, wg).then_inc(wg_in, 16)
            for q in range(1, PIECES):
                load_x0(q)
            load_half(we_rows, 0, 1)
            sp.dma_start(wt2_all[:, :, :], wt2.partition_broadcast(P)).then_inc(wt2_in, 16)
            with sp.Fori(0, CHUNKS - 1) as c:
                chunk(c, last=False)
            chunk(CHUNKS - 1, last=True)
            sp.wait_ge(gathered, CHUNKS)
            sp.dma_start(out, results[:, :]).then_inc(stored, 16)
            sp.wait_ge(stored, 16)

        def low_of(eng, low, high, value, q):
            return eng.tensor_tensor(low[:, q * KP:(q + 1) * KP, :], value,
                                     high[:, q * KP:(q + 1) * KP, :].bitcast(F32), ALU.subtract)

        def raw_piece(q):
            at = q * KP % KH
            return raw[q * KP // KH][:, at:at + KP, :]

        @block.gpsimd
        def _(pool):
            nc.gpsimd.memset(wg_split[:, :, 2 * GATES:].bitcast(F32), 0.0).then_inc(wg_zero, 1)
            nc.gpsimd.memset(ident[:, :], 0.0).then_inc(ident_zero, 1)
            pool.wait_ge(ident_zero, 1)
            nc.gpsimd.affine_select(out=ident[:, :], in_=ident[:, :], compare_op=ALU.not_equal, fill=1.0,
                                    base=0, pattern=[[-1, 2 * GATES]], channel_multiplier=1).then_inc(ident_made, 1)

            def slab_lows(s, b):
                for q in range(PIECES):
                    pool.wait_ge(high_made, s * PIECES + q + 1)
                    low_of(nc.gpsimd, slab_low[b], slab_high[b], raw_piece(q), q).then_inc(low_made, 1)

            def chunk_lows(c):
                with pool.Fori(0, STEPS // 2) as i:
                    for b in range(2):
                        slab_lows(c * STEPS + i * 2 + b, b)

            with pool.Fori(0, CHUNKS - 1) as c:
                chunk_lows(c)
                for q in range(PIECES):
                    pool.wait_ge(x_high_made, (c + 1) * PIECES + q + 1)
                    low_of(nc.gpsimd, x_low, x_high, raw_piece(q), q).then_inc(x_low_made, 1)
            chunk_lows(CHUNKS - 1)

        @block.scalar
        def _(act):
            def high_of(high, value, q):
                return nc.scalar.activation(high[:, q * KP:(q + 1) * KP, :], value, ACT.Copy)

            def half_loaded(h, n):
                act.wait_ge(raw_in[h], n * 16)

            def slab_highs(c, j, b, halves=(0, 1)):
                for h in halves:
                    half_loaded(h, c * (STEPS + 1) + j + 1)
                    for q in range(h * 2, h * 2 + 2):
                        high_of(slab_high[b], raw_piece(q), q).then_inc(high_made, 1)

            def next_x_highs(c, h):
                half_loaded(h, (c + 1) * (STEPS + 1))
                for q in range(h * 2, h * 2 + 2):
                    high_of(x_high, raw_piece(q), q).then_inc(x_high_made, 1)

            def relu(c, j, i):
                act.wait_ge(unit_done, c * UNITS + j * TILES + i + 1)
                nc.scalar.activation(z[i][:, :], z[i][:, :], ACT.Relu).then_inc(relu_made, 1)

            def round_turned(c, u):
                act.wait_ge(unit_done, c * UNITS + EXPERT_STEPS * TILES + u - 1)
                act.wait_ge(blocks_in[u % RING], (c * (TURNS // RING) + u // RING + 1) * (P // B) * 16)
                nc.scalar.activation(gt_high[u % 2][:, :, :].rearrange("p k (q i) -> p q k i", i=B),
                                     gt_raw[u % RING][:, :, :, :], ACT.Copy).then_inc(gt_high_made, 1)

            def experts(c):
                act.wait_ge(chunk_begun, c + 1)
                slab_highs(c, 1, 1)
                act.wait_ge(shifted_made, c + 1)
                nc.scalar.activation(expd[:, :, :], shifted[:, :, :], ACT.Exp).then_inc(expd_made, 1)
                for i in range(TILES):
                    relu(c, 0, i)
                with act.Fori(0, EXPERTS - 1) as e:
                    for half in range(HALVES):
                        j = e * HALVES + half + 1
                        act.wait_ge(unit_done, c * UNITS + j * TILES)
                        slab_highs(c, j + 1, half)
                        for i in range(TILES):
                            relu(c, j, i)
                j = EXPERT_STEPS - 1
                act.wait_ge(unit_done, c * UNITS + j * TILES)
                slab_highs(c, j + 1, 0)
                for i in range(TILES):
                    relu(c, j, i)
                    if i == TILES - 2:
                        round_turned(c, 0)

            def towers(c, last):
                for u in range(TURNS):
                    if u + 1 < TURNS:
                        round_turned(c, u + 1)
                    j = EXPERT_STEPS + u // TILES
                    if u % TILES == 0 and j + 1 < STEPS:
                        act.wait_ge(unit_done, c * UNITS + j * TILES)
                        slab_highs(c, j + 1, (j + 1) % 2)
                    if not last and u in X_HIGHS:
                        next_x_highs(c, X_HIGHS.index(u))
                    if not last and u in FIRST_SLAB_HIGHS:
                        slab_highs(c + 1, 0, 0, halves=(FIRST_SLAB_HIGHS.index(u),))

            def x0_highs(q):
                act.wait_ge(x0_in[q], 16)
                high_of(x_high, x0_raw[:, q * KP:(q + 1) * KP, :], q).then_inc(x_high_made, 1)

            x0_highs(0)
            act.wait_ge(slab0_in, 16)
            high_of(slab_high[0], raw_piece(0), 0).then_inc(high_made, 1)
            half_loaded(0, 1)
            high_of(slab_high[0], raw_piece(1), 1).then_inc(high_made, 1)
            act.wait_ge(wg_in, 16)
            nc.scalar.activation(wg_split[:, :, 0:GATES], wg_raw, ACT.Copy).then_inc(wg_high_made, 1)
            for q in range(1, PIECES):
                x0_highs(q)
            slab_highs(0, 0, 0, halves=(1,))
            with act.Fori(0, CHUNKS - 1) as c:
                experts(c)
                towers(c, last=False)
            experts(CHUNKS - 1)
            towers(CHUNKS - 1, last=True)

        @block.tensor
        def _(pe):
            def product(i, k, left_high, left_low, b):
                right_high, right_low = slab_high[b][:, k, :], slab_low[b][:, k, :]
                first = nc.tensor.matmul(z[i][:, :], left_high, right_high, start=(k == 0), stop=False)
                nc.tensor.matmul(z[i][:, :], left_high, right_low, start=False, stop=False)
                last = nc.tensor.matmul(z[i][:, :], left_low, right_high, start=False, stop=(k == KT - 1))
                return first, last

            def expert_product(i, k, b):
                rows = slice(i * P, (i + 1) * P)
                return product(i, k, x_high[:, k, rows], x_low[:, k, rows], b)

            def expert_unit(i, b):
                for k in range(KT):
                    _, last = expert_product(i, k, b)
                last.then_inc(unit_done, 1)

            def tower_unit(i, b):
                for k in range(KT):
                    _, last = product(i, k, gt_high[i % 2][:, k, :], gt_low[i % 2][:, k, :], b)
                last.then_inc(unit_done, 1)

            def slab_split(c, j, q=PIECES - 1):
                pe.wait_ge(low_made, (c * STEPS + j) * PIECES + q + 1)

            def x_split(c, q):
                pe.wait_ge(x_low_made, c * PIECES + q + 1)

            def bank_free(c, j, i):
                pe.wait_ge(unit_read, c * UNITS + j * TILES + i + 1)

            def gate_parts(c):
                x_split(c, PIECES - 1)
                for k in range(KT):
                    nc.tensor.matmul(parts_ps[:, :], wg_split[:, k, :], x_high[:, k, :], start=(k == 0), stop=False)
                    last = nc.tensor.matmul(parts_ps[:, :], wg_split[:, k, :], x_low[:, k, :],
                                            start=False, stop=(k == KT - 1))
                last.then_inc(parts_done, 1)

            def gate_logits(c):
                pe.wait_ge(parts_copied, c + 1)
                for i in range(TILES):
                    last = nc.tensor.matmul(logits_ps[:, i * TASKS:(i + 1) * TASKS, :], parts[:, i, :], fold[:, :],
                                            start=True, stop=True)
                last.then_inc(logits_done, 1)

            def first_step(c):
                for q in range(PIECES):
                    x_split(c, q)
                    slab_split(c, 0, q)
                    for i in range(TILES):
                        if q == 0:
                            bank_free(c, 0, i)
                        for k in range(q * KP, (q + 1) * KP):
                            first, last = expert_product(i, k, 0)
                            if (i, k) == (0, 0):
                                first.then_inc(chunk_begun, 1)
                        if q == PIECES - 1:
                            last.then_inc(unit_done, 1)
                    if q == 0:
                        gate_parts(c)
                    if q == 1:
                        gate_logits(c)

            pe.wait_ge(wg_zero, 1)
            pe.wait_ge(wg_low_made, 1)
            pe.wait_ge(fold_made, 1)
            with pe.Fori(0, CHUNKS) as c:
                first_step(c)
                with pe.Fori(0, EXPERTS - 1) as e:
                    for half in range(HALVES):
                        j = e * HALVES + half + 1
                        slab_split(c, j)
                        for i in range(TILES):
                            bank_free(c, j, i)
                            expert_unit(i, (half + 1) % 2)
                j = EXPERT_STEPS - 1
                slab_split(c, j)
                for i in range(TILES):
                    bank_free(c, j, i)
                    expert_unit(i, j % 2)
                for t in range(TASKS):
                    slab_split(c, EXPERT_STEPS + t)
                    for i in range(TILES):
                        pe.wait_ge(gt_low_made, c * TURNS + t * TILES + i + 1)
                        bank_free(c, EXPERT_STEPS + t, i)
                        tower_unit(i, t % 2)

        @block.vector
        def _(dve):
            LINKS = 4

            def wide(v):
                return v[:, :].rearrange("p (g o) -> p g o", o=1).to_broadcast([P, TURNS, EXPERTS])

            def softmax(c):
                dve.wait_ge(parts_done, c + 1)
                nc.vector.tensor_copy(parts, parts_ps[0:2 * GATES, :].rearrange("g (i r) -> g i r", r=P)
                                      ).then_inc(parts_copied, 1)
                dve.wait_ge(logits_done, c + 1)
                nc.vector.tensor_reduce(top[:, :], logits_ps[:, :, :], AX_X, ALU.max).then_inc(chain, 1)
                dve.wait_ge(chain, c * LINKS + 1)
                nc.vector.tensor_tensor(shifted[:, :, :], logits_ps[:, :, :], wide(top),
                                        ALU.subtract).then_inc(shifted_made, 1)
                dve.wait_ge(expd_made, c + 1)
                nc.vector.tensor_reduce(total[:, :], expd[:, :, :], AX_X, ALU.add).then_inc(chain, 1)
                dve.wait_ge(chain, c * LINKS + 2)
                nc.vector.reciprocal(inv[:, :], total[:, :]).then_inc(chain, 1)
                dve.wait_ge(chain, c * LINKS + 3)
                nc.vector.tensor_tensor(gate[:, :, :], expd[:, :, :], wide(inv), ALU.mult).then_inc(chain, 1)
                dve.wait_ge(chain, c * LINKS + 4)

            def add_expert(c, j, e, half, i, first=False):
                dve.wait_ge(relu_made, c * EXPERT_STEPS * TILES + j * TILES + i + 1)
                if not first:
                    dve.wait_ge(unit_read, c * UNITS + (j - HALVES + 1) * TILES + i + 1)
                for t in range(TASKS):
                    acc = gated[:, i, t, half * N:(half + 1) * N]
                    g = gate[:, i * TASKS + t, bass.ds(e, 1)]
                    if first:
                        last = nc.vector.tensor_scalar(acc, z[i][:, :], g, None, ALU.mult)
                    else:
                        last = nc.vector.scalar_tensor_tensor(out=acc, in0=z[i][:, :], scalar=g, in1=acc,
                                                              op0=ALU.mult, op1=ALU.add)
                last.then_inc(unit_read, 1)

            def turn_blocks(c, u, halves=HALVES, first=0):
                if u < TILES:
                    dve.wait_ge(unit_read, c * UNITS + (EXPERT_STEPS - HALVES + first + halves) * TILES + u + 1)
                part = gated[:, u % TILES, u // TILES, first * N:(first + halves) * N]
                return nc.vector.transpose(part, part)

            def low_turned(c, u):
                dve.wait_ge(gt_high_made, c * TURNS + u + 1)
                rows = "p k (q i) -> p q k i"
                nc.vector.tensor_tensor(gt_low[u % 2][:, :, :].rearrange(rows, i=B), gt_raw[u % RING][:, :, :, :],
                                        gt_high[u % 2][:, :, :].bitcast(F32).rearrange(rows, i=B),
                                        ALU.subtract).then_inc(gt_low_made, 1)

            def head(c, t, i):
                dve.wait_ge(unit_done, c * UNITS + (EXPERT_STEPS + t) * TILES + i + 1)
                nc.vector.scalar_tensor_tensor(out=z[i][:, :], in0=z[i][:, :], scalar=0.0, in1=wt2_all[:, t, :],
                                               op0=ALU.max, op1=ALU.mult,
                                               accum_out=result[:, i * TASKS + t:i * TASKS + t + 1]
                                               ).then_inc(unit_read, 1)

            nc.vector.memset(results[:, :], 0.0).then_inc(unit_read, TILES)
            dve.wait_ge(ident_made, 1)
            nc.vector.tensor_tensor(fold[:, :], ident[0:2 * GATES, 0:GATES], ident[0:2 * GATES, GATES:2 * GATES],
                                    ALU.add).then_inc(fold_made, 1)

            def x0_low(q):
                dve.wait_ge(x_high_made, q + 1)
                low_of(nc.vector, x_low, x_high, x0_raw[:, q * KP:(q + 1) * KP, :], q).then_inc(x_low_made, 1)

            x0_low(0)
            dve.wait_ge(wg_high_made, 1)
            nc.vector.tensor_tensor(wg_split[:, :, GATES:2 * GATES], wg_raw,
                                    wg_split[:, :, 0:GATES].bitcast(F32), ALU.subtract).then_inc(wg_low_made, 1)
            for q in range(1, PIECES):
                x0_low(q)
            dve.wait_ge(wt2_in, 16)
            with dve.Fori(0, CHUNKS) as c:
                softmax(c)
                for half in range(HALVES):
                    for i in range(TILES):
                        add_expert(c, half, 0, half, i, first=True)
                with dve.Fori(1, EXPERTS - 1) as e:
                    for half in range(HALVES):
                        for i in range(TILES):
                            add_expert(c, e * HALVES + half, e, half, i)
                for i in range(TILES):
                    add_expert(c, EXPERT_STEPS - 2, EXPERTS - 1, 0, i)
                    turn_blocks(c, i, halves=1, first=0)
                for i in range(TILES):
                    add_expert(c, EXPERT_STEPS - 1, EXPERTS - 1, 1, i)
                    turn_blocks(c, i, halves=1, first=1).then_inc(turned, 1)
                    if i >= 2:
                        low_turned(c, i - 2)
                for u in (TILES, TILES + 1):
                    turn_blocks(c, u).then_inc(turned, 1)
                for u in range(TURNS):
                    if u + 6 < TURNS:
                        turn_blocks(c, u + 6).then_inc(turned, 1)
                    head(c, u // TILES, u % TILES)
                    if u + 2 < TURNS:
                        low_turned(c, u + 2)
                dve.wait_ge(unit_read, (c + 1) * UNITS + TILES)
                nc.vector.tensor_copy(results[:, bass.ds(c * TURNS, TURNS)], result[:, :]).then_inc(gathered, 1)


def kernel(r_x, L0_rec_We, L0_rec_Wg, L0_rec_Wt1, L0_rec_Wt2):
    import numpy as np
    import concourse.bacc as bacc
    from concourse.bass_utils import run_bass_kernel_spmd

    rows, width = np.shape(r_x)
    experts, hidden, _ = np.shape(L0_rec_We)
    tasks, tower, _ = np.shape(L0_rec_Wt1)
    kt, ht, chunks, halves = width // 128, hidden // 128, rows // 512, hidden // 512

    arrays = {
        "x": np.asarray(r_x).reshape(chunks, 512, kt, 128).transpose(0, 3, 2, 1),
        "we": np.asarray(L0_rec_We).reshape(experts * halves, 512, kt, 128).transpose(0, 3, 2, 1),
        "wg": np.asarray(L0_rec_Wg).reshape(tasks * experts, kt, 128).transpose(2, 1, 0),
        "wt1": np.asarray(L0_rec_Wt1).reshape(tasks, tower, 4, ht, 32).transpose(0, 2, 4, 3, 1
                                              ).reshape(tasks, 128, ht, tower),
        "wt2": np.asarray(L0_rec_Wt2),
    }
    arrays = {n: np.ascontiguousarray(a) for n, a in arrays.items()}
    nc = bacc.Bacc("TRN2", target_bir_lowering=False, num_devices=1,
                   dynamic_dma_scratch_size=1024)
    args = [nc.dram_tensor(n, a.shape, mybir.dt.from_np(a.dtype), kind="ExternalInput").ap()
            for n, a in arrays.items()]
    out = nc.dram_tensor("out", (128, rows // 128 * tasks), F32, kind="ExternalOutput").ap()
    by_name = dict(zip(arrays, args))
    mmoe_kernel(nc, by_name["x"], by_name["we"], by_name["wg"], by_name["wt1"], by_name["wt2"], out)
    got = run_bass_kernel_spmd(nc, [arrays], core_ids=[0]).results[0]["out"]
    return got.reshape(128, rows // 128, tasks).transpose(1, 0, 2).reshape(rows, tasks)
```
